# Optimizing a Trainium2 kernel written in Bass

```python
import numpy as np
import jax
import jax.numpy as jnp

def _softmax(x, axis=-1):
    return jax.nn.softmax(x, axis=axis)
def _gelu(x):
    return jax.nn.gelu(x, approximate=True)
def _silu(x):
    return jax.nn.silu(x)
def _sigmoid(x):
    return jax.nn.sigmoid(x)
def _layernorm(x, axis=-1, eps=1e-5):
    m = jnp.mean(x, axis=axis, keepdims=True)
    v = jnp.var(x, axis=axis, keepdims=True)
    return (x - m) / jnp.sqrt(v + eps)
def _scatter_add(tgt, idx, src, axis=0):
    return tgt.at[idx].add(src)
def _segment_sum(src, seg, n):
    return jax.ops.segment_sum(src, seg, n)

kernel_name = 'mk_adj_resnorm_d2_adj_768_4b7732'

def setup_inputs(seed: int = 0):
    np.random.seed(seed)
    _w = jnp.asarray
    def _rec_inputs():
        import jax
        import jax.numpy as jnp
        _gk = jax.random.key(seed)
        x = -0.0005963 + 1.001 * jax.random.normal(jax.random.fold_in(_gk, 1), (128, 64, 768), jnp.float32)
        _a = jax.random.bernoulli(jax.random.fold_in(_gk, 2), 0.125, (128, 64, 64))
        _a = jnp.logical_or(_a, jnp.swapaxes(_a, -1, -2))
        _a = jnp.logical_or(_a, jnp.eye(64, dtype=bool))
        adj = _a
        return x, adj
    x, adj = _rec_inputs()
    def _L0_gnn_setup():
        import jax, jax.numpy as jnp
        import numpy as np
        ATT_HEAD = 12
        IN_DIM = 768
        OUT_DIM = IN_DIM // ATT_HEAD
        LEAKY_ALPHA = 0.2
        B, N = (8, 512)
        key = jax.random.key(seed)
        ks = jax.random.split(key, 8)
        feat_in = jax.random.normal(ks[0], (B, N, IN_DIM), dtype=jnp.float32)
        adj = jax.random.randint(ks[1], (B, N, N), 0, 2) > 0
        lim_W = float(np.sqrt(6.0 / (IN_DIM + OUT_DIM)))
        W = jax.random.uniform(ks[2], (ATT_HEAD, IN_DIM, OUT_DIM), minval=-lim_W, maxval=lim_W, dtype=jnp.float32)
        b = jnp.zeros((OUT_DIM,), dtype=jnp.float32)
        lim_w = float(np.sqrt(6.0 / (OUT_DIM + 1)))
        w_src = jax.random.uniform(ks[3], (ATT_HEAD, OUT_DIM, 1), minval=-lim_w, maxval=lim_w, dtype=jnp.float32)
        w_dst = jax.random.uniform(ks[4], (ATT_HEAD, OUT_DIM, 1), minval=-lim_w, maxval=lim_w, dtype=jnp.float32)
        std_H = float(np.sqrt(2.0 / (IN_DIM + IN_DIM)))
        H_w = jax.random.normal(ks[5], (IN_DIM, IN_DIM), dtype=jnp.float32) * std_H
        H_b = jax.random.normal(ks[6], (IN_DIM,), dtype=jnp.float32) * 0.01
        return {'feat_in': feat_in, 'adj': adj, 'W': W, 'b': b, 'w_src': w_src, 'w_dst': w_dst, 'H_w': H_w, 'H_b': H_b}
    _L0_gnn_all = _L0_gnn_setup()
    _L0_gnn_in = {k: v for k, v in _L0_gnn_all.items() if k in ('W', 'b', 'w_src', 'w_dst', 'H_w', 'H_b', )}
    del _L0_gnn_all

    def _L1_gnn_setup():
        import jax, jax.numpy as jnp
        import numpy as np
        B, S, H = (4, 2048, 768)
        NUM_HEADS = 6
        HEAD_SIZE = H // NUM_HEADS
        NEG = -9000000000000000.0

        def _heads(x):
            b, s, _ = x.shape
            return x.reshape(b, s, NUM_HEADS, HEAD_SIZE).transpose(0, 2, 1, 3)
        key = jax.random.key(seed)
        ks = jax.random.split(key, 10)
        seq_inputs = jax.random.normal(ks[0], (B, S, H), dtype=jnp.float32)
        gm = jax.random.randint(ks[1], (B, S, S), 0, 2) > 0
        graph_mask = gm | jnp.eye(S, dtype=bool)[None]
        sc = 1.0 / np.sqrt(H)
        Wq = jax.random.normal(ks[2], (H, H), dtype=jnp.float32) * sc
        bq = jnp.zeros((H,), dtype=jnp.float32)
        Wk = jax.random.normal(ks[3], (H, H), dtype=jnp.float32) * sc
        bk = jnp.zeros((H,), dtype=jnp.float32)
        Wv = jax.random.normal(ks[4], (H, H), dtype=jnp.float32) * sc
        bv = jnp.zeros((H,), dtype=jnp.float32)
        Wf = jax.random.normal(ks[5], (H, H), dtype=jnp.float32) * sc
        bf = jnp.zeros((H,), dtype=jnp.float32)
        return {'seq_inputs': seq_inputs, 'Wq': Wq, 'bq': bq, 'Wk': Wk, 'bk': bk, 'Wv': Wv, 'bv': bv, 'Wf': Wf, 'bf': bf, 'graph_mask': graph_mask}
    _L1_gnn_all = _L1_gnn_setup()
    _L1_gnn_in = {k: v for k, v in _L1_gnn_all.items() if k in ('Wq', 'bq', 'Wk', 'bk', 'Wv', 'bv', 'Wf', 'bf', )}
    del _L1_gnn_all

    return {
        "x": x,
        "adj": adj,
        "L0_gnn_W": _L0_gnn_in["W"],
        "L0_gnn_b": _L0_gnn_in["b"],
        "L0_gnn_w_src": _L0_gnn_in["w_src"],
        "L0_gnn_w_dst": _L0_gnn_in["w_dst"],
        "L0_gnn_H_w": _L0_gnn_in["H_w"],
        "L0_gnn_H_b": _L0_gnn_in["H_b"],
        "L1_gnn_Wq": _L1_gnn_in["Wq"],
        "L1_gnn_bq": _L1_gnn_in["bq"],
        "L1_gnn_Wk": _L1_gnn_in["Wk"],
        "L1_gnn_bk": _L1_gnn_in["bk"],
        "L1_gnn_Wv": _L1_gnn_in["Wv"],
        "L1_gnn_bv": _L1_gnn_in["bv"],
        "L1_gnn_Wf": _L1_gnn_in["Wf"],
        "L1_gnn_bf": _L1_gnn_in["bf"],
    }

def reference(x, adj, L0_gnn_W, L0_gnn_b, L0_gnn_w_src, L0_gnn_w_dst, L0_gnn_H_w, L0_gnn_H_b, L1_gnn_Wq, L1_gnn_bq, L1_gnn_Wk, L1_gnn_bk, L1_gnn_Wv, L1_gnn_bv, L1_gnn_Wf, L1_gnn_bf):
    import jax
    import jax.numpy as jnp
    def _L0_gnn_ref(feat_in, adj, W, b, w_src, w_dst, H_w, H_b):
        import jax, jax.numpy as jnp
        import numpy as np
        ATT_HEAD = 12
        IN_DIM = 768
        OUT_DIM = IN_DIM // ATT_HEAD
        LEAKY_ALPHA = 0.2
        B, N = (8, 512)
        h = jnp.einsum('bnd,ade->bane', feat_in, W)
        th = jnp.tanh(h)
        attn_src = jnp.einsum('bane,aeo->bano', th, w_src)
        attn_dst = jnp.einsum('bane,aeo->bano', th, w_dst)
        attn = attn_src + jnp.swapaxes(attn_dst, 2, 3)
        attn = jnp.where(attn >= 0, attn, LEAKY_ALPHA * attn)
        mask = ~adj[:, None, :, :]
        attn = jnp.where(mask, jnp.float32(-999.0), attn)
        attn = jax.nn.softmax(attn, axis=-1)
        feat_out = jnp.einsum('banm,bame->bane', attn, h) + b
        feat_out = jnp.swapaxes(feat_out, 1, 2).reshape(feat_in.shape[0], feat_in.shape[1], -1)
        feat_out = jax.nn.elu(feat_out)
        gate = jax.nn.sigmoid(feat_in @ H_w.T + H_b)
        return gate * feat_out + (1.0 - gate) * feat_in

    def _L1_gnn_ref(seq_inputs, Wq, bq, Wk, bk, Wv, bv, Wf, bf, graph_mask):
        import jax, jax.numpy as jnp
        import numpy as np
        B, S, H = (4, 2048, 768)
        NUM_HEADS = 6
        HEAD_SIZE = H // NUM_HEADS
        NEG = -9000000000000000.0

        def _heads(x):
            b, s, _ = x.shape
            return x.reshape(b, s, NUM_HEADS, HEAD_SIZE).transpose(0, 2, 1, 3)
        q = _heads(seq_inputs @ Wq + bq)
        k = _heads(seq_inputs @ Wk + bk)
        v = _heads(seq_inputs @ Wv + bv)
        scores = jnp.einsum('bhqd,bhkd->bhqk', q, k) / np.sqrt(HEAD_SIZE)
        bias = jnp.where(graph_mask, 0.0, NEG)[:, None]
        probs = jax.nn.softmax(scores + bias, axis=-1)
        ctx = jnp.einsum('bhqk,bhkd->bhqd', probs, v)
        ctx = ctx.transpose(0, 2, 1, 3).reshape(seq_inputs.shape[0], seq_inputs.shape[1], H)
        return ctx @ Wf + bf

    x = _layernorm(x + _L0_gnn_ref(x, adj, L0_gnn_W, L0_gnn_b, L0_gnn_w_src, L0_gnn_w_dst, L0_gnn_H_w, L0_gnn_H_b), axis=-1)
    x = _layernorm(x + _L1_gnn_ref(x, L1_gnn_Wq, L1_gnn_bq, L1_gnn_Wk, L1_gnn_bk, L1_gnn_Wv, L1_gnn_bv, L1_gnn_Wf, L1_gnn_bf, adj), axis=-1)
    return x


_drawn_inputs = setup_inputs


def setup_inputs(seed=0):
    import zlib

    import numpy as np

    out = dict(_drawn_inputs(seed))
    spreads = {'L0_gnn_b': (0.0, 0.1),
     'L1_gnn_bq': (0.0, 0.286),
     'L1_gnn_bk': (0.0, 2.0),
     'L1_gnn_bv': (0.0, 0.1),
     'L1_gnn_bf': (0.0, 0.1)}
    factors = {'L0_gnn_H_b': 33.86}
    for name, (base, spread) in spreads.items():
        noise = np.random.default_rng([zlib.crc32(name.encode()), seed]).standard_normal(out[name].shape)
        drawn = base * np.exp(spread * noise) if base else spread * noise
        out[name] = jnp.asarray(drawn.astype(out[name].dtype))
    for name, factor in factors.items():
        out[name] = (out[name] * factor).astype(out[name].dtype)
    return out
```

```python
from contextlib import ExitStack

import concourse.bass as bass
from concourse import mybir

F32 = mybir.dt.float32
F32R = mybir.dt.float32r
U8 = mybir.dt.uint8
I32 = mybir.dt.int32
ALU = mybir.AluOpType
ACT = mybir.ActivationFunctionType
AX_X = mybir.AxisListType.X

P = 128
NODES = 64
D = 768
KC = D // P
HALF = D // 2
HEADS0, E0 = 12, 64
HEADS1, E1 = 6, 128
SCALE1 = float(1.0 / (E1 ** 0.5))
LEAKY = 0.2
MASKED0 = -999.0
MASKED1 = -9000000000000000.0
EPS = 1e-5
RSQRT_SEED = float(0x5F3759DF)
LAYER0_UNROLL = 4
LAYER1_UNROLL = 2
GT = 2
GN = GT * P


def banks(ps):
    return ps[:, :, 0:HALF]


def halves(sb):
    return sb.rearrange("p (b n) -> p b n", b=2)


def per_head(sb, heads):
    return sb.rearrange("p (a m) -> p a m", a=heads)


def over(col, heads, n):
    return col.unsqueeze(2).to_broadcast([col.shape[0], heads, n])


def rsqrt_steps(dve, var, y, q, seed, eps, done):
    r = seed.bitcast(F32)
    done(dve.tensor_scalar(var, var, eps, None, ALU.add))
    done(dve.tensor_single_scalar(seed, var.bitcast(I32), 1, ALU.arith_shift_right))
    done(dve.tensor_scalar(y.bitcast(I32), seed, -1.0, RSQRT_SEED, ALU.mult, ALU.add))
    for _ in range(2):
        done(dve.tensor_scalar(q, y, y, var, ALU.mult, ALU.mult))
        done(dve.tensor_scalar(r, q, 0.375, -1.25, ALU.mult, ALU.add))
        done(dve.tensor_scalar(r, r, q, 1.875, ALU.mult, ALU.add))
        done(dve.tensor_scalar(y, y, r, None, ALU.mult))


RSQRT_STEPS = 11


def split_weights(nc, block, sources, stage, w_hi, w_lo, sem):
    units = [(m, c) for m in range(len(sources)) for c in range(KC)]
    slots = stage.shape[1]
    loaded = [sem(f"w_loaded{s}") for s in range(slots)]
    hi_done = sem("w_hi_done")
    lo_done = sem("w_lo_done")

    def load(sp):
        for n, (m, c) in enumerate(units):
            if n >= slots:
                sp.wait_ge(lo_done, n - slots + 1)
            sp.dma_start(stage[:, n % slots, :], sources[m][c * P:(c + 1) * P, :]).then_inc(loaded[n % slots], 16)

    def hi(act):
        for n, (m, c) in enumerate(units):
            act.wait_ge(loaded[n % slots], 16 * (n // slots + 1))
            act.copy(w_hi[:, m, c, :], stage[:, n % slots, :]).then_inc(hi_done, 1)

    def lo(dve):
        for n, (m, c) in enumerate(units):
            dve.wait_ge(hi_done, n + 1)
            dve.tensor_tensor(w_lo[:, m, c, :], stage[:, n % slots, :], w_hi[:, m, c, :].bitcast(F32),
                              ALU.subtract).then_inc(lo_done, 1)

    return load, hi, lo, lo_done, len(units)


def product(pe, out, left, right):
    terms = [(c, a, b) for c in range(KC) for a, b in ((0, 0), (0, 1), (1, 0))]
    for n, (c, a, b) in enumerate(terms):
        ins = pe.matmul(out, left[a][c], right[b][c], start=(n == 0), stop=(n == len(terms) - 1))
    return ins


def identity(pool, ident, ones, sem_ones, sem_ident):
    pool.wait_ge(sem_ones, 1)
    pool.affine_select(out=ident, in_=ones, compare_op=ALU.is_equal, fill=0.0, base=0,
                       pattern=[[-1, P]], channel_multiplier=1).then_inc(sem_ident, 1)


def layer0(nc, x, adj, W, b, w_src, w_dst, Ht, H_b, x1):
    NT = x.shape[0] // P
    x_t = x.rearrange("(t p) d -> t p d", p=P)
    adj_t = adj.rearrange("(t p) m -> t p m", p=P)
    x1_t = x1.rearrange("(t p) d -> t p d", p=P)

    with ExitStack() as ctx:
        def sb(name, shape, dt=F32):
            return ctx.enter_context(nc.sbuf_tensor("L0_" + name, shape, dt))

        def sem(name):
            return ctx.enter_context(nc.semaphore("L0_" + name))

        w_hi = sb("w_hi", [P, 2, KC, D], F32R)
        w_lo = sb("w_lo", [P, 2, KC, D], F32R)
        stage = sb("stage", [P, 4, D])
        x_tok = sb("x_tok", [P, 4, D])
        adj_u8 = sb("adj_u8", [P, 4, NODES], U8)
        not_adj = sb("not_adj", [P, 2, NODES], U8)
        xT_hi = sb("xT_hi", [P, 2, KC, P], F32R)
        xT_lo = sb("xT_lo", [P, 2, KC, P], F32R)
        h_tok = sb("h_tok", [P, 2, D])
        th = sb("th", [P, D])
        th_dst = sb("th_dst", [P, D])
        th_src = sb("th_src", [P, D])
        dst = sb("dst", [P, HEADS0])
        src = sb("src", [P, 2, HEADS0])
        dst_diag = sb("dst_diag", [P, D])
        logits = sb("logits", [P, D])
        neg_max = sb("neg_max", [P, HEADS0])
        probs = sb("probs", [P, D])
        row_sum = sb("row_sum", [P, 2, HEADS0])
        row_inv = sb("row_inv", [P, HEADS0])
        probsT = sb("probsT", [P, HEADS0, P])
        att = sb("att", [P, D])
        feat = sb("feat", [P, D])
        gate = sb("gate", [P, 2, D])
        x1_out = sb("x1_out", [P, 2, D])
        stats = sb("stats", [P, 2, 6])
        mean_var = sb("mean_var", [P, 2])
        rstd = sb("rstd", [P, 1])
        shift = sb("shift", [P, 1])
        tmp = sb("tmp", [P, 1])
        seed = sb("seed", [P, 1], I32)
        ident = sb("ident", [P, P])
        ones = sb("ones", [P, P])
        same_graph = sb("same_graph", [P, P])
        node_of = sb("node_of", [P, NODES])
        masked = sb("masked", [P, 1])
        b_less1 = sb("b_less1", [P, E0])
        wsrc_all = sb("wsrc_all", [P, D])
        wdst_all = sb("wdst_all", [P, D])
        Hb_all = sb("Hb_all", [P, D])

        def psum(name):
            return ctx.enter_context(nc.psum_tensor("L0_" + name, [P, 2, 512], F32))

        ps_h = psum("ps_h")
        ps_g = psum("ps_g")
        ps_xa = psum("ps_xa")
        ps_pt = psum("ps_pt")

        x_in = [sem(f"x_in{s}") for s in range(4)]
        x1_stored = [sem(f"x1_stored{s}") for s in range(2)]
        consts_in, memsets, ident_ok, graph_ok, bd_zero = (
            sem(n) for n in ("consts_in", "memsets", "ident_ok", "graph_ok", "bd_zero"))
        xT_done, hi_done, lo_done = sem("xT_done"), sem("xT_hi_done"), sem("xT_lo_done")
        h_done, g_done, bc_done, pt_done, pv_done = (
            sem(n) for n in ("h_done", "g_done", "bc_done", "pt_done", "pv_done"))
        tanh_done, h_copied, mask_done = sem("tanh_done"), sem("h_copied"), sem("mask_done")
        thdst_done, thsrc_done, dst_done, src_done, diag_done = (
            sem(n) for n in ("thdst_done", "thsrc_done", "dst_done", "src_done", "diag_done"))
        sum_done, leaky_done, masked_done, max_done, exp_done = (
            sem(n) for n in ("sum_done", "leaky_done", "masked_done", "max_done", "exp_done"))
        ptc_done, inv_done, att_done, attb_done = (
            sem(n) for n in ("ptc_done", "inv_done", "att_done", "attb_done"))
        elu_done, elu_sum, delta_done, x2_done, relu_done, z_done, gate_done = (
            sem(n) for n in ("elu_done", "elu_sum", "delta_done", "x2_done", "relu_done", "z_done", "gate_done"))
        gated_done, y_done, stat_done, mv_done, newton, shift_done, norm_done = (
            sem(n) for n in ("gated_done", "y_done", "stat_done", "mv_done", "newton", "shift_done", "norm_done"))

        block = ctx.enter_context(nc.Block())
        w_load, w_split_hi, w_split_lo, w_ready, w_units = split_weights(
            nc, block, [W, Ht], stage, w_hi, w_lo, sem)

        def steps(eng, step, last):
            U = LAYER0_UNROLL
            for T in range(U):
                step(T, T, lambda d: 0 <= T + d < NT)
            with eng.Fori(1, NT // U - 1) as i:
                for u in range(U):
                    step(i * U + u, u, lambda d: True)
            for T in range(NT - U, last):
                step(T, T % U, lambda d: 0 <= T + d < NT)

        def x_use(T, u):
            return (T - u) * 8 + 32

        def x1_use(T, u):
            return (T - 4 - u % 2) * 8 + 16

        def copy_block(act, parity, g):
            rows = slice(parity * NODES, (parity + 1) * NODES)
            s = slice(g * NODES, (g + 1) * NODES)
            out = probsT[s, :, s].rearrange("p (b c two) n -> p b c two n", b=2, two=2)[:, :, :, parity, :]
            src_ = banks(ps_pt)[rows, :, :].rearrange("p b (c n) -> p b c n", c=KC // 2)[:, :, :, s]
            return act.copy(out, src_)

        @block.sync
        def _(sp):
            for t in range(4):
                sp.dma_start(x_tok[:, t, :], x_t[t]).then_inc(x_in[t], 16)
                sp.dma_start(adj_u8[:, t, :], adj_t[t]).then_inc(x_in[t], 16)
            w_load(sp)
            for out, row in ((b_less1, b), (wsrc_all, w_src), (wdst_all, w_dst), (Hb_all, H_b)):
                sp.dma_start(out[:, :], row.partition_broadcast(P)).then_inc(consts_in, 16)

            def step(T, u, has):
                if has(4):
                    sp.wait_ge(delta_done, T + 1)
                    sp.wait_ge(x2_done, T + 1)
                    sp.dma_start(x_tok[:, u, :], x_t[T + 4]).then_inc(x_in[u], 16)
                    sp.dma_start(adj_u8[:, u, :], adj_t[T + 4]).then_inc(x_in[u], 16)
                if has(-1):
                    sp.wait_ge(norm_done, T)
                    sp.dma_start(x1_t[T - 1], x1_out[:, (u + 1) % 2, :]).then_inc(x1_stored[(u + 1) % 2], 16)

            steps(sp, step, NT + 1)
            for s in range(2):
                sp.wait_ge(x1_stored[s], 16 * (NT // 2))

        @block.gpsimd
        def _(pool):
            pool.memset(ones[:, :], 1.0).then_inc(memsets, 1)
            identity(pool, ident[:, :], ones[:, :], memsets, ident_ok)
            pool.wait_ge(graph_ok, 6)
            pool.wait_ge(consts_in, 64)
            pool.tensor_scalar(b_less1[:, :], b_less1[:, :], -1.0, None, ALU.add).then_inc(memsets, 1)
            pool.wait_ge(memsets, 2)

            def step(T, u, has):
                if has(-2):
                    pool.wait_ge(att_done, T - 1)
                    pool.tensor_tensor(per_head(att[:, :], HEADS0), per_head(att[:, :], HEADS0),
                                       b_less1[:, :].unsqueeze(1).to_broadcast([P, HEADS0, E0]),
                                       ALU.add).then_inc(attb_done, 1)
                if has(0):
                    pool.wait_ge(tanh_done, T + 1)
                    if has(-1):
                        pool.wait_ge(src_done, T)
                    pool.tensor_tensor(th_src[:, :], th[:, :], wsrc_all[:, :], ALU.mult).then_inc(thsrc_done, 1)
                    pool.wait_ge(dst_done, T + 1)
                    if has(-1):
                        pool.wait_ge(bc_done, T)
                    pool.tensor_tensor(
                        per_head(dst_diag[:, :], HEADS0), over(dst[:, :], HEADS0, NODES),
                        node_of[:, :].unsqueeze(1).to_broadcast([P, HEADS0, NODES]), ALU.mult).then_inc(diag_done, 1)
                if has(-2):
                    pool.wait_ge(elu_sum, T - 1)
                    pool.tensor_tensor(feat[:, :], feat[:, :], x_tok[:, (u - 2) % 4, :],
                                       ALU.subtract).then_inc(delta_done, 1)
                    pool.wait_ge(delta_done, T - 1)
                    pool.wait_ge(gate_done, 2 * (T - 1))
                    pool.tensor_tensor(feat[:, :], feat[:, :], gate[:, u % 2, :], ALU.mult).then_inc(gated_done, 1)
                    pool.wait_ge(gated_done, T - 1)
                    pool.wait_ge(x2_done, T - 1)
                    pool.tensor_tensor(x1_out[:, u % 2, :], x1_out[:, u % 2, :], feat[:, :], ALU.add).then_inc(y_done, 1)

            steps(pool, step, NT + 2)

        @block.scalar
        def _(act):
            act.wait_ge(bd_zero, 1)

            def transposed_hi(u):
                act.copy(xT_hi[:, u % 2, :, :].rearrange("p (b c) n -> p b (c n)", b=2),
                         banks(ps_xa)).then_inc(hi_done, 1)

            act.wait_ge(xT_done, 1)
            transposed_hi(0)
            w_split_hi(act)

            def exps(T, u, heads):
                for a in heads:
                    act.activation(per_head(probs[:, :], HEADS0)[:, a, :], per_head(logits[:, :], HEADS0)[:, a, :],
                                   ACT.Exp, bias=neg_max[:, a:a + 1],
                                   accum_out=row_sum[:, (u - 1) % 2, a:a + 1]).then_inc(exp_done, 1)

            def step(T, u, has):
                if has(1):
                    act.wait_ge(xT_done, T + 2)
                    if has(-1):
                        act.wait_ge(g_done, T)
                    transposed_hi(u + 1)
                if has(-1):
                    act.wait_ge(max_done, T)
                    if has(-2):
                        act.wait_ge(pt_done, T - 1)
                    exps(T, u, range(HEADS0 // 2))
                if has(0):
                    act.wait_ge(h_done, T + 1)
                    if has(-1):
                        act.wait_ge(thdst_done, T)
                        act.wait_ge(thsrc_done, T)
                    act.activation(halves(th[:, :]), banks(ps_h), ACT.Tanh).then_inc(tanh_done, 1)
                if has(-1):
                    exps(T, u, range(HEADS0 // 2, HEADS0))
                if has(0):
                    if has(-2):
                        act.wait_ge(pv_done, T - 1)
                    act.copy(halves(h_tok[:, u % 2, :]), banks(ps_h)).then_inc(h_copied, 1)
                    act.wait_ge(x_in[u], x_use(T, u))
                    if has(-2):
                        act.wait_ge(masked_done, T - 1)
                    act.activation(not_adj[:, u % 2, :], adj_u8[:, u, :], ACT.Copy, scale=-1.0,
                                   bias=1.0).then_inc(mask_done, 1)
                if has(-2):
                    act.wait_ge(attb_done, T - 1)
                    if has(-3):
                        act.wait_ge(y_done, T - 2)
                    act.activation(feat[:, :], att[:, :], ACT.Relu, scale=-1.0, bias=-1.0).then_inc(relu_done, 1)
                    act.wait_ge(relu_done, T - 1)
                    act.activation(feat[:, :], feat[:, :], ACT.Exp, scale=-1.0).then_inc(elu_done, 1)
                if has(-1):
                    act.wait_ge(pt_done, T)
                    for parity in range(2):
                        for g in range(2):
                            ins = copy_block(act, parity, g)
                    ins.then_inc(ptc_done, 1)
                if has(-2):
                    if not isinstance(T, int) or T >= 4:
                        act.wait_ge(x1_stored[u % 2], x1_use(T, u))
                    act.mul(x1_out[:, u % 2, :], x_tok[:, (u - 2) % 4, :], 2.0).then_inc(x2_done, 1)
                if has(-1):
                    act.wait_ge(z_done, T)
                    g = gate[:, (u - 1) % 2, :]
                    act.activation(g, g, ACT.Tanh, scale=0.5).then_inc(gate_done, 1)
                    act.wait_ge(gate_done, 2 * T - 1)
                    act.activation(g, g, ACT.Copy, scale=0.5, bias=0.5).then_inc(gate_done, 1)
                if has(-3):
                    act.wait_ge(shift_done, T - 2)
                    out = x1_out[:, (u + 1) % 2, :]
                    act.activation(out, out, ACT.Identity, scale=rstd[:, 0:1],
                                   bias=shift[:, 0:1]).then_inc(norm_done, 1)

            steps(act, step, NT + 3)

        @block.vector
        def _(dve):
            def transposed_lo(u):
                dve.tensor_tensor(xT_lo[:, u % 2, :, :].rearrange("p (b c) n -> p b (c n)", b=2), banks(ps_xa),
                                  xT_hi[:, u % 2, :, :].bitcast(F32).rearrange("p (b c) n -> p b (c n)", b=2),
                                  ALU.subtract).then_inc(lo_done, 1)

            dve.memset(probsT[:, :, :], 0.0).then_inc(bd_zero, 1)
            dve.memset(same_graph[:, :], 0.0).then_inc(graph_ok, 1)
            dve.wait_ge(graph_ok, 1)
            for g in range(2):
                dve.memset(same_graph[g * NODES:(g + 1) * NODES, g * NODES:(g + 1) * NODES], 1.0).then_inc(graph_ok, 1)
            dve.memset(masked[:, :], MASKED0).then_inc(graph_ok, 1)
            dve.wait_ge(ident_ok, 1)
            for g in range(2):
                s = slice(g * NODES, (g + 1) * NODES)
                dve.tensor_copy(node_of[s, :], ident[s, s]).then_inc(graph_ok, 1)
            dve.wait_ge(bd_zero, 1)
            dve.wait_ge(hi_done, 1)
            transposed_lo(0)
            w_split_lo(dve)
            dve.wait_ge(consts_in, 64)
            dve.wait_ge(graph_ok, 4)

            def step(T, u, has):
                if has(-2):
                    dve.wait_ge(exp_done, HEADS0 * (T - 1))
                    dve.reciprocal(row_inv[:, :], row_sum[:, u % 2, :]).then_inc(inv_done, 1)
                    dve.wait_ge(inv_done, T - 1)
                    dve.wait_ge(pv_done, T - 1)
                    dve.tensor_tensor(
                        att[:, :].rearrange("p (b a e) -> p b a e", b=2, e=E0),
                        banks(ps_xa).rearrange("p b (a e) -> p b a e", e=E0),
                        row_inv[:, :].rearrange("p (b a) -> p b a", b=2).unsqueeze(3)
                        .to_broadcast([P, 2, HEADS0 // 2, E0]), ALU.mult).then_inc(att_done, 1)
                if has(-1):
                    dve.wait_ge(bc_done, T)
                    dve.wait_ge(src_done, T)
                    if has(-2):
                        dve.wait_ge(exp_done, HEADS0 * (T - 1))
                    dve.tensor_tensor(
                        logits[:, :].rearrange("p (b a m) -> p b a m", b=2, m=NODES),
                        banks(ps_pt).rearrange("p b (a m) -> p b a m", m=NODES),
                        src[:, (u - 1) % 2, :].rearrange("p (b a) -> p b a", b=2).unsqueeze(3)
                        .to_broadcast([P, 2, HEADS0 // 2, NODES]), ALU.add).then_inc(sum_done, 1)
                    dve.wait_ge(sum_done, T)
                    dve.scalar_tensor_tensor(out=logits[:, :], in0=logits[:, :], scalar=LEAKY, in1=logits[:, :],
                                             op0=ALU.mult, op1=ALU.max).then_inc(leaky_done, 1)
                    dve.wait_ge(graph_ok, 4)
                    dve.wait_ge(leaky_done, T)
                    dve.wait_ge(mask_done, T)
                    dve.copy_predicated(
                        per_head(logits[:, :], HEADS0),
                        not_adj[:, (u - 1) % 2, :].unsqueeze(1).to_broadcast([P, HEADS0, NODES]),
                        masked[:, 0:1].unsqueeze(2).to_broadcast([P, HEADS0, NODES])).then_inc(masked_done, 1)
                    dve.wait_ge(masked_done, T)
                    dve.tensor_reduce(neg_max[:, :], per_head(logits[:, :], HEADS0), AX_X, ALU.max,
                                      negate=True).then_inc(max_done, 1)
                if has(1):
                    dve.wait_ge(hi_done, T + 2)
                    transposed_lo(u + 1)
                if has(0):
                    dve.wait_ge(tanh_done, T + 1)
                    dve.tensor_tensor(th_dst[:, :], th[:, :], wdst_all[:, :], ALU.mult).then_inc(thdst_done, 1)
                    dve.wait_ge(thdst_done, T + 1)
                    if has(-1):
                        dve.wait_ge(diag_done, T)
                    dve.tensor_reduce(dst[:, :], per_head(th_dst[:, :], HEADS0), AX_X, ALU.add).then_inc(dst_done, 1)
                    dve.wait_ge(thsrc_done, T + 1)
                    dve.tensor_reduce(src[:, u % 2, :], per_head(th_src[:, :], HEADS0), AX_X,
                                      ALU.add).then_inc(src_done, 1)
                if has(-2):
                    dve.wait_ge(elu_done, T - 1)
                    dve.scalar_tensor_tensor(out=feat[:, :], in0=att[:, :], scalar=-1.0, in1=feat[:, :],
                                             op0=ALU.max, op1=ALU.add).then_inc(elu_sum, 1)
                if has(-3):
                    out = x1_out[:, (u + 1) % 2, :]
                    dve.wait_ge(y_done, T - 2)
                    for s in range(2):
                        ins = dve.bn_stats(stats[:, s, :], out[:, s * HALF:(s + 1) * HALF])
                    ins.then_inc(stat_done, 1)
                    dve.wait_ge(consts_in, 64)
                    dve.wait_ge(stat_done, T - 2)
                    dve.bn_aggr(mean_var[:, :], stats[:, :, :]).then_inc(mv_done, 1)
                    dve.wait_ge(mv_done, T - 2)
                    if has(-4):
                        dve.wait_ge(norm_done, T - 3)
                    n = [0]

                    def done(ins):
                        n[0] += 1
                        ins.then_inc(newton, 1)
                        dve.wait_ge(newton, (T - 3) * RSQRT_STEPS + n[0])

                    rsqrt_steps(dve, mean_var[:, 1:2], rstd[:, :], tmp[:, :], seed[:, :], EPS, done)
                    assert n[0] == RSQRT_STEPS
                    dve.tensor_scalar(shift[:, :], mean_var[:, 0:1], rstd[:, 0:1], -1.0, ALU.mult,
                                      ALU.mult).then_inc(shift_done, 1)
                if has(0):
                    dve.wait_ge(g_done, T + 1)
                    if has(-2):
                        dve.wait_ge(gated_done, T - 1)
                    dve.tensor_tensor(halves(gate[:, u % 2, :]), banks(ps_g), halves(Hb_all[:, :]),
                                      ALU.add).then_inc(z_done, 1)

            steps(dve, step, NT + 3)

        @block.tensor
        def _(pe):
            pe.wait_ge(ident_ok, 1)
            pe.wait_ge(graph_ok, 3)

            def transpose_x(T, u):
                pe.wait_ge(x_in[u % 4], x_use(T, u % 4))
                for c in range(KC):
                    ins = pe.transpose(banks(ps_xa)[:, c // 3, (c % 3) * P:(c % 3 + 1) * P],
                                       x_tok[:, u % 4, c * P:(c + 1) * P], ident[:, :])
                ins.then_inc(xT_done, 1)

            def project(ps, matrix, half, u):
                cols = slice(half * HALF, (half + 1) * HALF)
                return product(pe, ps[:, half, 0:HALF],
                               [[xT[:, u % 2, c, :] for c in range(KC)] for xT in (xT_hi, xT_lo)],
                               [[w[:, matrix, c, cols] for c in range(KC)] for w in (w_hi, w_lo)])

            transpose_x(0, 0)
            pe.wait_ge(w_ready, w_units)

            def step(T, u, has):
                if has(0):
                    pe.wait_ge(lo_done, T + 1)
                    if has(-1):
                        pe.wait_ge(h_copied, T)
                    project(ps_h, 0, 0, u)
                if has(1):
                    if has(-2):
                        pe.wait_ge(att_done, T - 1)
                    transpose_x(T + 1, u + 1)
                if has(0):
                    project(ps_h, 0, 1, u).then_inc(h_done, 1)
                    if has(-1):
                        pe.wait_ge(z_done, T)
                    project(ps_g, 1, 0, u)
                if has(-1):
                    pe.wait_ge(exp_done, HEADS0 * T)
                    for c in range(KC):
                        ins = pe.transpose(banks(ps_pt)[:, c // 3, (c % 3) * P:(c % 3 + 1) * P],
                                           probs[:, c * P:(c + 1) * P], ident[:, :])
                    ins.then_inc(pt_done, 1)
                if has(0):
                    project(ps_g, 1, 1, u).then_inc(g_done, 1)
                if has(-1):
                    pe.wait_ge(ptc_done, T)
                if has(0):
                    pe.wait_ge(diag_done, T + 1)
                    for s in range(2):
                        ins = pe.matmul(ps_pt[:, s, 0:HALF], same_graph[:, :],
                                        dst_diag[:, s * HALF:(s + 1) * HALF], start=True, stop=True)
                    ins.then_inc(bc_done, 1)
                if has(-1):
                    if has(1):
                        pe.wait_ge(lo_done, T + 2)
                    for a in range(HEADS0):
                        half, at = a // 6, (a % 6) * E0
                        ins = pe.matmul(ps_xa[:, half, at:at + E0], probsT[:, a, :],
                                        h_tok[:, (u - 1) % 2, a * E0:(a + 1) * E0], start=True, stop=True)
                    ins.then_inc(pv_done, 1)

            steps(pe, step, NT + 1)


def layer1(nc, x1, adj, Wq, bq, Wk, bk, Wv, bv, Wf, bf, out):
    NG = x1.shape[0] // GN
    PAIRS = HEADS1 // 2
    PN = 2 * GT
    x1_g = x1.rearrange("(g t p) d -> g p t d", t=GT, p=P)
    out_g = out.rearrange("(g t p) d -> g p t d", t=GT, p=P)
    adj_g = adj.rearrange("(g t p) m -> g p t m", t=GT, p=P)

    with ExitStack() as ctx:
        def sb(name, shape, dt=F32):
            return ctx.enter_context(nc.sbuf_tensor("L1_" + name, shape, dt))

        def sem(name):
            return ctx.enter_context(nc.semaphore("L1_" + name))

        w_hi = sb("w_hi", [P, 4, KC, D], F32R)
        w_lo = sb("w_lo", [P, 4, KC, D], F32R)
        x_tok = sb("x_tok", [P, 2, GT, D])
        adj_u8 = sb("adj_u8", [P, 2, GT, NODES], U8)
        mask = sb("mask", [P, 2, GT, NODES])
        xT_hi = sb("xT_hi", [P, KC, GN], F32R)
        xT_lo = sb("xT_lo", [P, KC, GN], F32R)
        v_tok = sb("v_tok", [P, GT, D])
        qT = sb("qT", [P, 2, 2, GN])
        kT = sb("kT", [P, 2, GN])
        logits = sb("logits", [P, PN, NODES])
        neg_max = sb("neg_max", [P, PN])
        probs = sb("probs", [P, PN, NODES])
        row_sum = sb("row_sum", [P, PN])
        row_inv = sb("row_inv", [P, PN])
        probsT = sb("probsT", [P, PN, P])
        cT_hi = sb("cT_hi", [P, KC, GN], F32R)
        cT_lo = sb("cT_lo", [P, KC, GN], F32R)
        bq_col, bk_col, bv_col = (sb(n, [P, HEADS1]) for n in ("bq_col", "bk_col", "bv_col"))
        bf_all = sb("bf_all", [P, D])
        stats = sb("stats", [P, GT, 2, 6])
        mean_var = sb("mean_var", [P, GT, 2])
        rstd = sb("rstd", [P, GT])
        tmp = sb("tmp", [P, GT])
        seed = sb("seed", [P, GT], I32)
        ident = sb("ident", [P, P])
        ones = sb("ones", [P, P])

        def psum(name):
            return ctx.enter_context(nc.psum_tensor("L1_" + name, [P, 512], F32))

        ps_q, ps_k, ps_s, ps_pt, ps_c = (psum(n) for n in ("ps_q", "ps_k", "ps_s", "ps_pt", "ps_c"))
        ps_a = [psum(f"ps_a{i}") for i in range(3)]
        v_bank = [0, 1, 2, 0]
        o_bank = [1, 2, 0, 1]
        ps_x = [ps_q, ps_k, ps_s]

        x_in = [sem(f"x_in{s}") for s in range(2)]
        stored = [sem(f"stored{s}") for s in range(2)]
        consts_in, memsets, ident_ok, bd_zero = (sem(n) for n in ("consts_in", "memsets", "ident_ok", "bd_zero"))
        xT_done, hi_done, lo_done = sem("xT_done"), sem("xT_hi_done"), sem("xT_lo_done")
        v_done, v_copied, o_done, o_added = (sem(n) for n in ("v_done", "v_copied", "o_done", "o_added"))
        q_done, q_copied, k_done, k_copied, s_done = (
            sem(n) for n in ("q_done", "q_copied", "k_done", "k_copied", "s_done"))
        mask_done, logit_done, max_done, exp_done, inv_done, probs_done = (
            sem(n) for n in ("mask_done", "logit_done", "max_done", "exp_done", "inv_done", "probs_done"))
        pt_done, ptc_act, ptc_dve, c_done, c_hi, c_lo = (
            sem(n) for n in ("pt_done", "ptc_act", "ptc_dve", "c_done", "c_hi", "c_lo"))
        biased, stat_done, mv_done, newton, norm_done = (
            sem(n) for n in ("biased", "stat_done", "mv_done", "newton", "norm_done"))

        block = ctx.enter_context(nc.Block())
        w_load, w_split_hi, w_split_lo, w_ready, w_units = split_weights(
            nc, block, [Wq, Wk, Wv, Wf], x_tok.rearrange("p s t d -> p (s t) d"), w_hi, w_lo, sem)

        def groups(eng, body):
            U = LAYER1_UNROLL
            for G in range(U):
                body(G, G, G == 0, False)
            with eng.Fori(1, NG // U - 1) as i:
                for s in range(U):
                    body(i * U + s, s, False, False)
            for G in range(NG - U, NG):
                body(G, G % U, False, G == NG - 1)

        def x_use(G, s):
            return (G - s) * 16 + 32

        @block.sync
        def _(sp):
            w_load(sp)
            sp.dma_start(bf_all[:, :], bf.partition_broadcast(P)).then_inc(consts_in, 16)
            for col, bias in ((bq_col, bq), (bk_col, bk), (bv_col, bv)):
                sp.dma_start(col[:, :], bias).then_inc(consts_in, 16)
            sp.wait_ge(w_ready, w_units)
            for G in range(2):
                sp.dma_start(x_tok[:, G], x1_g[G]).then_inc(x_in[G], 16)
                sp.dma_start(adj_u8[:, G], adj_g[G]).then_inc(x_in[G], 16)

            def body(G, s, first, last):
                more = not isinstance(G, int) or G + 2 < NG
                sp.wait_ge(norm_done, GT * (G + 1))
                sp.dma_start(out_g[G], x_tok[:, s]).then_inc(stored[s], 16)
                if more:
                    sp.dma_start(adj_u8[:, s], adj_g[G + 2]).then_inc(x_in[s], 16)
                    sp.wait_ge(stored[s], (G - s) * 8 + 16)
                    sp.dma_start(x_tok[:, s], x1_g[G + 2]).then_inc(x_in[s], 16)

            groups(sp, body)
            for s in range(2):
                sp.wait_ge(stored[s], 16 * (NG // 2))

        @block.gpsimd
        def _(pool):
            pool.memset(ones[:, :], 1.0).then_inc(memsets, 1)
            identity(pool, ident[:, :], ones[:, :], memsets, ident_ok)
            pool.wait_ge(consts_in, 64)

            def body(G, s, first, last):
                pool.wait_ge(xT_done, 3 * (G + 1))
                for t in range(GT):
                    pool.tensor_tensor(x_tok[:, s, t], x_tok[:, s, t], bf_all[:, :], ALU.add).then_inc(biased, 1)

            groups(pool, body)

        def copy_block(copy, t, g, signal):
            s = slice(g * NODES, (g + 1) * NODES)
            out_ = probsT[s, :, s].rearrange("p (h t) n -> p h t n", t=GT)[:, :, t, :]
            src_ = ps_pt[t * NODES:(t + 1) * NODES, 0:2 * P].rearrange("p (h n) -> p h n", h=2)[:, :, s]
            copy(out_, src_).then_inc(signal, 1)

        @block.scalar
        def _(act):
            w_split_hi(act)
            act.wait_ge(bd_zero, 1)
            act.wait_ge(consts_in, 64)

            def transposed_hi(G):
                for n in range(3):
                    act.wait_ge(xT_done, 3 * G + n + 1)
                    act.copy(xT_hi[:, 2 * n:2 * n + 2, :],
                             ps_x[n][:, :].rearrange("p (c n) -> p c n", c=2)).then_inc(hi_done, 1)

            def heads_out(dst, ps, col, j, signal):
                for h in range(2):
                    a = 2 * j + h
                    act.activation(dst[h], ps[:, h * GN:(h + 1) * GN], ACT.Identity,
                                   bias=col[:, a:a + 1]).then_inc(signal, 1)

            def q_out(G, j):
                act.wait_ge(q_done, PAIRS * G + j + 1)
                heads_out([qT[:, j % 2, h, :] for h in range(2)], ps_q, bq_col, j, q_copied)

            def k_out(G, j):
                act.wait_ge(k_done, PAIRS * G + j + 1)
                heads_out([kT[:, h, :] for h in range(2)], ps_k, bk_col, j, k_copied)

            def exps(G, j, first):
                act.wait_ge(max_done, PAIRS * G + j + 1)
                for k in range(PN):
                    act.activation(probs[:, k, :], logits[:, k, :], ACT.Exp, bias=neg_max[:, k:k + 1],
                                   accum_out=row_sum[:, k:k + 1]).then_inc(exp_done, 1)

            def probs_out(G, j):
                act.wait_ge(pt_done, PAIRS * G + j + 1)
                for g in range(2):
                    copy_block(act.copy, 0, g, ptc_act)

            def context_hi(G, j):
                act.wait_ge(c_done, PAIRS * G + j + 1)
                heads_out([cT_hi[:, 2 * j + h, :] for h in range(2)], ps_c, bv_col, j, c_hi)

            transposed_hi(0)

            def body(G, s, first, last):
                act.wait_ge(x_in[s], x_use(G, s))
                if not first:
                    act.wait_ge(logit_done, 2 * PAIRS * G)
                act.activation(mask[:, s], adj_u8[:, s], ACT.Copy, scale=-MASKED1, bias=MASKED1).then_inc(mask_done, 1)
                for n in range(2 * GT):
                    act.wait_ge(v_done, 2 * GT * G + n + 1)
                    act.copy(v_tok[:, n // 2, (n % 2) * HALF:(n % 2 + 1) * HALF],
                             ps_a[v_bank[n]][:, 0:HALF]).then_inc(v_copied, 1)
                q_out(G, 0)
                k_out(G, 0)
                q_out(G, 1)
                exps(G, 0, first)
                k_out(G, 1)
                probs_out(G, 0)
                q_out(G, 2)
                exps(G, 1, False)
                context_hi(G, 0)
                k_out(G, 2)
                probs_out(G, 1)
                exps(G, 2, False)
                context_hi(G, 1)
                probs_out(G, 2)
                context_hi(G, 2)
                if not last:
                    transposed_hi(G + 1)

            groups(act, body)

        @block.vector
        def _(dve):
            dve.memset(probsT[:, :, :], 0.0).then_inc(bd_zero, 1)
            w_split_lo(dve)
            dve.wait_ge(bd_zero, 1)
            dve.wait_ge(consts_in, 64)

            def transposed_lo(G):
                for n in range(3):
                    dve.wait_ge(hi_done, 3 * G + n + 1)
                    dve.tensor_tensor(xT_lo[:, 2 * n:2 * n + 2, :],
                                      ps_x[n][:, :].rearrange("p (c n) -> p c n", c=2),
                                      xT_hi[:, 2 * n:2 * n + 2, :].bitcast(F32), ALU.subtract).then_inc(lo_done, 1)

            def logits_of(G, j, s):
                dve.wait_ge(s_done, PAIRS * G + j + 1)
                if j == 0:
                    dve.wait_ge(mask_done, G + 1)
                for g in range(2):
                    r = slice(g * NODES, (g + 1) * NODES)
                    dve.scalar_tensor_tensor(
                        out=logits[r].rearrange("p (h t) m -> p h t m", t=GT),
                        in0=ps_s[r, :].rearrange("p (h t m) -> p h t m", h=2, t=GT)[:, :, :, r],
                        scalar=SCALE1, in1=mask[r, s].unsqueeze(1).to_broadcast([NODES, 2, GT, NODES]),
                        op0=ALU.mult, op1=ALU.add).then_inc(logit_done, 1)
                dve.wait_ge(logit_done, 2 * (PAIRS * G + j + 1))
                dve.tensor_reduce(neg_max[:, :], logits[:, :, :], AX_X, ALU.max, negate=True).then_inc(max_done, 1)

            def normalise(G, j):
                dve.wait_ge(exp_done, PN * (PAIRS * G + j + 1))
                dve.reciprocal(row_inv[:, :], row_sum[:, :]).then_inc(inv_done, 1)
                dve.wait_ge(inv_done, PAIRS * G + j + 1)
                dve.tensor_tensor(probs[:, :, :], probs[:, :, :], over(row_inv[:, :], PN, NODES),
                                  ALU.mult).then_inc(probs_done, 1)

            def probs_out(G, j):
                dve.wait_ge(pt_done, PAIRS * G + j + 1)
                for g in range(2):
                    copy_block(dve.tensor_copy, 1, g, ptc_dve)

            def context_lo(G, j):
                dve.wait_ge(c_hi, 2 * (PAIRS * G + j + 1))
                for h in range(2):
                    a = 2 * j + h
                    dve.scalar_tensor_tensor(out=cT_lo[:, a, :], in0=ps_c[:, h * GN:(h + 1) * GN],
                                             scalar=bv_col[:, a:a + 1], in1=cT_hi[:, a, :].bitcast(F32),
                                             op0=ALU.add, op1=ALU.subtract).then_inc(c_lo, 1)

            transposed_lo(0)

            def body(G, s, first, last):
                logits_of(G, 0, s)
                normalise(G, 0)
                probs_out(G, 0)
                logits_of(G, 1, s)
                normalise(G, 1)
                context_lo(G, 0)
                probs_out(G, 1)
                logits_of(G, 2, s)
                normalise(G, 2)
                context_lo(G, 1)
                probs_out(G, 2)
                context_lo(G, 2)
                if not last:
                    transposed_lo(G + 1)
                dve.wait_ge(biased, GT * (G + 1))
                for n in range(2 * GT):
                    t, cols = n // 2, slice((n % 2) * HALF, (n % 2 + 1) * HALF)
                    dve.wait_ge(o_done, 2 * GT * G + n + 1)
                    dve.tensor_tensor(x_tok[:, s, t, cols], ps_a[o_bank[n]][:, 0:HALF], x_tok[:, s, t, cols],
                                      ALU.add).then_inc(o_added, 1)
                    dve.wait_ge(o_added, 2 * GT * G + n + 1)
                    ins = dve.bn_stats(stats[:, t, n % 2, :], x_tok[:, s, t, cols])
                ins.then_inc(stat_done, 1)
                dve.wait_ge(consts_in, 64)
                dve.wait_ge(stat_done, G + 1)
                for t in range(GT):
                    dve.bn_aggr(mean_var[:, t, :], stats[:, t]).then_inc(mv_done, 1)
                dve.wait_ge(mv_done, GT * (G + 1))
                n = [0]

                def done(ins):
                    n[0] += 1
                    ins.then_inc(newton, 1)
                    dve.wait_ge(newton, G * GT * RSQRT_STEPS + n[0])

                for t in range(GT):
                    c = slice(t, t + 1)
                    rsqrt_steps(dve, mean_var[:, t, 1:2], rstd[:, c], tmp[:, c], seed[:, c], EPS, done)
                assert n[0] == GT * RSQRT_STEPS
                for t in range(GT):
                    dve.tensor_scalar(x_tok[:, s, t], x_tok[:, s, t], mean_var[:, t, 0:1], rstd[:, t:t + 1],
                                      ALU.subtract, ALU.mult).then_inc(norm_done, 1)

            groups(dve, body)

        @block.tensor
        def _(pe):
            def transpose_x(G, s):
                pe.wait_ge(x_in[s], x_use(G, s))
                for n in range(3):
                    for c in range(2):
                        for t in range(GT):
                            ins = pe.transpose(ps_x[n][:, c * GN + t * P:c * GN + (t + 1) * P],
                                               x_tok[:, s, t, (2 * n + c) * P:(2 * n + c + 1) * P], ident[:, :])
                    ins.then_inc(xT_done, 1)

            def nodes(T, t):
                return [[x[:, c, t * P:(t + 1) * P] for c in range(KC)] for x in T]

            def weights(matrix, cols):
                return [[w[:, matrix, c, cols] for c in range(KC)] for w in (w_hi, w_lo)]

            xT, cT = (xT_hi, xT_lo), (cT_hi, cT_lo)
            all_nodes = [[x[:, c, :] for c in range(KC)] for x in xT]

            def value(G, n, first):
                if n < 2:
                    if not first:
                        pe.wait_ge(o_added, 2 * GT * G - 1 + n)
                elif n == 3:
                    pe.wait_ge(v_copied, 2 * GT * G + 1)
                product(pe, ps_a[v_bank[n]][:, 0:HALF], nodes(xT, n // 2),
                        weights(2, slice((n % 2) * HALF, (n % 2 + 1) * HALF))).then_inc(v_done, 1)

            def query_or_key(matrix, ps, j, signal):
                for h in range(2):
                    a = 2 * j + h
                    ins = product(pe, ps[:, h * GN:(h + 1) * GN],
                                  weights(matrix, slice(a * E1, (a + 1) * E1)), all_nodes)
                ins.then_inc(signal, 1)

            def query(G, j):
                if j > 0:
                    pe.wait_ge(q_copied, 2 * (PAIRS * G + j))
                query_or_key(0, ps_q, j, q_done)

            def key(G, j):
                if j > 0:
                    pe.wait_ge(k_copied, 2 * (PAIRS * G + j))
                query_or_key(1, ps_k, j, k_done)

            def scores(G, j):
                pe.wait_ge(q_copied, 2 * (PAIRS * G + j + 1))
                pe.wait_ge(k_copied, 2 * (PAIRS * G + j + 1))
                for h in range(2):
                    for t in range(GT):
                        n = slice(t * P, (t + 1) * P)
                        ins = pe.matmul(ps_s[:, (h * GT + t) * P:(h * GT + t + 1) * P], qT[:, j % 2, h, n],
                                        kT[:, h, n], start=True, stop=True)
                ins.then_inc(s_done, 1)

            def transpose_probs(G, j):
                pe.wait_ge(probs_done, PAIRS * G + j + 1)
                for h in range(2):
                    ins = pe.transpose(ps_pt[:, h * P:(h + 1) * P],
                                       probs[:, h * GT:(h + 1) * GT, :].rearrange("p t m -> p (t m)"), ident[:, :])
                ins.then_inc(pt_done, 1)

            def context(G, j, first):
                pe.wait_ge(ptc_act, 2 * (PAIRS * G + j + 1))
                pe.wait_ge(ptc_dve, 2 * (PAIRS * G + j + 1))
                pe.wait_ge(v_copied, 2 * GT * (G + 1))
                if j > 0 or not first:
                    pe.wait_ge(c_lo, 2 * (PAIRS * G + j))
                for h in range(2):
                    for t in range(GT):
                        a = 2 * j + h
                        ins = pe.matmul(ps_c[:, h * GN + t * P:h * GN + (t + 1) * P],
                                        v_tok[:, t, a * E1:(a + 1) * E1], probsT[:, h * GT + t, :],
                                        start=True, stop=True)
                ins.then_inc(c_done, 1)

            def output(G, n, pair):
                if pair == 0:
                    if n < 3:
                        pe.wait_ge(v_copied, 2 * GT * G + n + 2)
                    else:
                        pe.wait_ge(o_added, 2 * GT * G + 1)
                pe.wait_ge(c_lo, 2 * (PAIRS * G + pair + 1))
                left = nodes(cT, n // 2)
                right = weights(3, slice((n % 2) * HALF, (n % 2 + 1) * HALF))
                for c in (2 * pair, 2 * pair + 1):
                    for k, (a, b) in enumerate(((0, 0), (0, 1), (1, 0))):
                        ins = pe.matmul(ps_a[o_bank[n]][:, 0:HALF], left[a][c], right[b][c],
                                        start=(c == 0 and k == 0), stop=(c == KC - 1 and k == 2))
                if pair == PAIRS - 1:
                    ins.then_inc(o_done, 1)

            pe.wait_ge(ident_ok, 1)
            pe.wait_ge(w_ready, w_units)
            transpose_x(0, 0)

            def body(G, s, first, last):
                pe.wait_ge(lo_done, 3 * (G + 1))
                for n in range(2 * GT):
                    value(G, n, first)
                query(G, 0)
                key(G, 0)
                query(G, 1)
                scores(G, 0)
                key(G, 1)
                transpose_probs(G, 0)
                query(G, 2)
                scores(G, 1)
                context(G, 0, first)
                key(G, 2)
                transpose_probs(G, 1)
                output(G, 0, 0)
                scores(G, 2)
                context(G, 1, first)
                output(G, 1, 0)
                output(G, 2, 0)
                transpose_probs(G, 2)
                output(G, 0, 1)
                output(G, 1, 1)
                context(G, 2, first)
                if not last:
                    transpose_x(G + 1, 1 - s)
                output(G, 2, 1)
                for n in range(3):
                    output(G, n, 2)
                for pair in range(PAIRS):
                    output(G, 3, pair)

            groups(pe, body)


def two_graph_layers(nc, x, adj, W0, b0, w_src, w_dst, H_t, H_b, Wq, bq, Wk, bk, Wv, bv, Wf, bf, out):
    x1 = nc.dram_tensor("x1_scratch", list(x.shape), F32).ap()
    layer0(nc, x, adj, W0, b0, w_src, w_dst, H_t, H_b, x1)
    layer1(nc, x1, adj, Wq, bq, Wk, bk, Wv, bv, Wf, bf, out)


def kernel(x, adj, L0_gnn_W, L0_gnn_b, L0_gnn_w_src, L0_gnn_w_dst, L0_gnn_H_w, L0_gnn_H_b, L1_gnn_Wq, L1_gnn_bq,
           L1_gnn_Wk, L1_gnn_bk, L1_gnn_Wv, L1_gnn_bv, L1_gnn_Wf, L1_gnn_bf):
    import numpy as np
    import concourse.bacc as bacc
    from concourse.bass_utils import run_bass_kernel_spmd

    B, N, _ = x.shape

    def head_columns(bias):
        return np.ascontiguousarray(np.asarray(bias).reshape(HEADS1, E1).T)

    arrays = {
        "x": np.asarray(x).reshape(B * N, D),
        "adj": np.asarray(adj).reshape(B * N, N),
        "W0": np.ascontiguousarray(np.asarray(L0_gnn_W).transpose(1, 0, 2)).reshape(D, D),
        "b0": np.asarray(L0_gnn_b),
        "w_src": np.asarray(L0_gnn_w_src).reshape(D),
        "w_dst": np.asarray(L0_gnn_w_dst).reshape(D),
        "H_t": np.ascontiguousarray(np.asarray(L0_gnn_H_w).T),
        "H_b": np.asarray(L0_gnn_H_b),
        "Wq": np.asarray(L1_gnn_Wq), "bq": head_columns(L1_gnn_bq),
        "Wk": np.asarray(L1_gnn_Wk), "bk": head_columns(L1_gnn_bk),
        "Wv": np.asarray(L1_gnn_Wv), "bv": head_columns(L1_gnn_bv),
        "Wf": np.asarray(L1_gnn_Wf), "bf": np.asarray(L1_gnn_bf),
    }
    nc = bacc.Bacc("TRN2", target_bir_lowering=False, num_devices=1)
    args = [nc.dram_tensor(n, a.shape, mybir.dt.from_np(a.dtype), kind="ExternalInput").ap()
            for n, a in arrays.items()]
    args.append(nc.dram_tensor("out", (B * N, D), F32, kind="ExternalOutput").ap())
    two_graph_layers(nc, *args)
    result = run_bass_kernel_spmd(nc, [arrays], core_ids=[0])
    return result.results[0]["out"].reshape(B, N, D)
```
